# Optimizing a Trainium2 kernel written in Bass

```python
import numpy as np
import jax
import jax.numpy as jnp

def _softmax(x, axis=-1):
    return jax.nn.softmax(x, axis=axis)

def _gelu(x):
    return jax.nn.gelu(x, approximate=True)

def _silu(x):
    return jax.nn.silu(x)

def _sigmoid(x):
    return jax.nn.sigmoid(x)

def _layernorm(x, axis=-1, eps=1e-05):
    m = jnp.mean(x, axis=axis, keepdims=True)
    v = jnp.var(x, axis=axis, keepdims=True)
    return (x - m) / jnp.sqrt(v + eps)

def _scatter_add(tgt, idx, src, axis=0):
    return tgt.at[idx].add(src)

def _segment_sum(src, seg, n):
    return jax.ops.segment_sum(src, seg, n)
kernel_name = 'mk_gnn_ffn_d1_gnn_r32_f92a8b'

def setup_inputs(seed: int=0):
    np.random.seed(seed)
    _w = jnp.asarray

    def _rec_inputs():
        import jax
        import jax.numpy as jnp
        _gk = jax.random.key(seed)
        x = -0.0003019 + 1 * jax.random.normal(jax.random.fold_in(_gk, 1), (10000, 1024), jnp.float32)
        src = jax.random.randint(jax.random.fold_in(_gk, 2), (5000,), 0, 10000, jnp.int32)
        dst = jnp.minimum((10000 * jax.random.uniform(jax.random.fold_in(_gk, 3), (5000,)) ** 2.0).astype(jnp.int32), 9999)
        _o = jnp.argsort(dst, stable=True)
        src = src[_o]
        dst = dst[_o]
        return (x, src, dst)
    x, src, dst = _rec_inputs()

    def _L0_gnn_setup():
        import jax, jax.numpy as jnp
        import numpy as np
        N = 625
        E = 10000
        D_IN = 1024
        D_OUT = 1024
        key = jax.random.key(seed)
        k1, k2, k3, k4 = jax.random.split(key, 4)
        x = jax.random.normal(k1, (N, D_IN), dtype=jnp.float32)
        edge_index = jax.random.randint(k2, (2, E), 0, N, dtype=jnp.int64)
        W = jax.random.normal(k3, (D_OUT, D_IN), dtype=jnp.float32) * (1.0 / np.sqrt(D_IN))
        b = jax.random.normal(k4, (D_OUT,), dtype=jnp.float32) * 0.01
        return {'x': x, 'edge_index': edge_index, 'W': W, 'b': b}
    _L0_gnn_all = _L0_gnn_setup()
    _L0_gnn_in = {k: v for k, v in _L0_gnn_all.items() if k in ('W', 'b')}
    del _L0_gnn_all

    def _L0_ffn_setup():
        import jax, jax.numpy as jnp
        import numpy as np
        B, S, D = (8, 128, 1024)
        E, R, K = (6, 16, 2)
        key = jax.random.key(seed)
        ks = jax.random.split(key, 9)
        sc = 0.02
        return {'x': jax.random.normal(ks[0], (B, S, D), jnp.float32), 'base_W': jax.random.normal(ks[1], (D, D), jnp.float32) * sc, 'base_b': jax.random.normal(ks[2], (D,), jnp.float32) * sc, 'shared_A': jax.random.normal(ks[3], (R, D), jnp.float32) * sc, 'shared_B': jax.random.normal(ks[4], (D, R), jnp.float32) * sc, 'routed_A': jax.random.normal(ks[5], (E, R, D), jnp.float32) * sc, 'routed_B': jax.random.normal(ks[6], (E, D, R), jnp.float32) * sc, 'router_W': jax.random.normal(ks[7], (E, D), jnp.float32) * sc, 'router_b': jax.random.normal(ks[8], (E,), jnp.float32) * sc}
    _L0_ffn_all = _L0_ffn_setup()
    _L0_ffn_in = {k: v for k, v in _L0_ffn_all.items() if k in ('base_W', 'base_b', 'shared_A', 'shared_B', 'routed_A', 'routed_B', 'router_W', 'router_b')}
    del _L0_ffn_all
    return {'x': x, 'src': src, 'dst': dst, 'L0_gnn_W': _L0_gnn_in['W'], 'L0_gnn_b': _L0_gnn_in['b'], 'L0_ffn_base_W': _L0_ffn_in['base_W'], 'L0_ffn_base_b': _L0_ffn_in['base_b'], 'L0_ffn_shared_A': _L0_ffn_in['shared_A'], 'L0_ffn_shared_B': _L0_ffn_in['shared_B'], 'L0_ffn_routed_A': _L0_ffn_in['routed_A'], 'L0_ffn_routed_B': _L0_ffn_in['routed_B'], 'L0_ffn_router_W': _L0_ffn_in['router_W'], 'L0_ffn_router_b': _L0_ffn_in['router_b']}

def reference(x, src, dst, L0_gnn_W, L0_gnn_b, L0_ffn_base_W, L0_ffn_base_b, L0_ffn_shared_A, L0_ffn_shared_B, L0_ffn_routed_A, L0_ffn_routed_B, L0_ffn_router_W, L0_ffn_router_b):
    import jax
    import jax.numpy as jnp

    def _L0_gnn_ref(x, edge_index, W, b):
        import jax, jax.numpy as jnp
        import numpy as np
        N = 625
        E = 10000
        D_IN = 1024
        D_OUT = 1024
        num_nodes = x.shape[0]
        self_idx = jnp.arange(num_nodes, dtype=edge_index.dtype)
        ei = jnp.concatenate([edge_index, jnp.stack([self_idx, self_idx], axis=0)], axis=1)
        row, col = (ei[0], ei[1])
        h = jnp.einsum('nd,od->no', x, W) + b
        deg = jnp.zeros((num_nodes,), dtype=h.dtype).at[row].add(1.0)
        deg_inv_sqrt = deg ** (-0.5)
        norm = deg_inv_sqrt[row] * deg_inv_sqrt[col]
        msg = norm[:, None] * h[col]
        out = jax.ops.segment_sum(msg, row, num_segments=num_nodes)
        return out

    def _L0_ffn_ref(x, base_W, base_b, shared_A, shared_B, routed_A, routed_B, router_W, router_b):
        import jax, jax.numpy as jnp
        import numpy as np
        B, S, D = (8, 128, 1024)
        E, R, K = (6, 16, 2)
        base_out = jax.lax.stop_gradient(jnp.einsum('bsi,oi->bso', x, base_W) + base_b)
        shared_out = jnp.einsum('bsr,or->bso', jnp.einsum('bsi,ri->bsr', x, shared_A), shared_B)
        logits = jnp.einsum('bsi,ei->bse', x, router_W) + router_b
        gate = jax.nn.softmax(logits, axis=-1)
        topk_w, topk_i = jax.lax.top_k(gate, K)
        sparse_w = jnp.sum(jax.nn.one_hot(topk_i, E, dtype=gate.dtype) * topk_w[..., None], axis=-2)
        sparse_w = sparse_w / (jnp.sum(sparse_w, axis=-1, keepdims=True) + 1e-06)
        h = jnp.einsum('bsi,eri->bser', x, routed_A)
        routed_outs = jnp.einsum('bser,eor->bseo', h, routed_B)
        routed_out = jnp.einsum('bseo,bse->bso', routed_outs, sparse_w)
        return base_out + shared_out + routed_out
    edge_index = jnp.stack([src, dst])
    x = x + _L0_gnn_ref(_layernorm(x, axis=-1), edge_index, L0_gnn_W, L0_gnn_b)
    x = x + _L0_ffn_ref(_layernorm(x, axis=-1)[None], L0_ffn_base_W, L0_ffn_base_b, L0_ffn_shared_A, L0_ffn_shared_B, L0_ffn_routed_A, L0_ffn_routed_B, L0_ffn_router_W, L0_ffn_router_b)[0]
    return x

_drawn_inputs = setup_inputs


def setup_inputs(seed=0):
    import zlib

    import numpy as np

    out = dict(_drawn_inputs(seed))
    spreads = {}
    factors = {'L0_gnn_b': 7.577,
     'L0_ffn_base_b': 4.218,
     'L0_ffn_router_W': 7.87,
     'L0_ffn_router_b': 200.0}
    for name, (base, spread) in spreads.items():
        noise = np.random.default_rng([zlib.crc32(name.encode()), seed]).standard_normal(out[name].shape)
        drawn = base * np.exp(spread * noise) if base else spread * noise
        out[name] = jnp.asarray(drawn.astype(out[name].dtype))
    for name, factor in factors.items():
        out[name] = (out[name] * factor).astype(out[name].dtype)
    return out
```

```python
from contextlib import ExitStack

import concourse.bass as bass
from concourse import mybir

F32 = mybir.dt.float32
F32R = mybir.dt.float32r
BF16 = mybir.dt.bfloat16
I32 = mybir.dt.int32
U32 = mybir.dt.uint32
ALU = mybir.AluOpType
ACT = mybir.ActivationFunctionType
AX = mybir.AxisListType

P = 128
N = 10000
D = 1024
E = 5000
TILES = -(-N // P)
NPAD = TILES * P
CHUNKS = -(-E // P)
EPAD = CHUNKS * P
KB = D // P
HALF = 512
EXPERTS, RANK, TOPK = 6, 16, 2
ROUTED = RANK
LOGITS = RANK * (EXPERTS + 1)
HCOLS = LOGITS + EXPERTS
BCOLS = HCOLS + D
CUTS = [0, 380, 760, BCOLS]
KLOW = LOGITS + 1
LN_EPS = 1e-5
GATE_EPS = 1e-6
GROUP = HALF // TILES
GROUPS = -(-CHUNKS // GROUP)
SPILLW = D + 1
FAR = 20000


class Chain:

    def __init__(self, sem, per):
        self.sem, self.per, self.tile, self.at = sem, per, 0, 0

    def start(self, tile):
        self.tile, self.at = tile, 0

    def link(self, eng, ins):
        self.at += 1
        ins.then_inc(self.sem, 1)
        eng.wait_ge(self.sem, self.tile * self.per + self.at)

    def end(self):
        assert self.at == self.per, (self.at, self.per)


class Step:

    def __init__(self, k, q):
        self.k, self.q, self.i = k, q, 2 * k + q

    def has(self, a):
        return not isinstance(self.i, int) or 0 <= self.i + a < TILES

    def tile(self, a):
        return self.i + a

    def par(self, a):
        return (self.q + a) % 2

    def half(self, a):
        return self.k + (self.q + a) // 2


def pipeline(eng, body, first, last):
    a, b = 2, TILES - 2
    b -= (b - a) % 2
    for i in range(first, a):
        body(Step(i // 2, i % 2))
    with eng.Fori(a // 2, b // 2) as k:
        body(Step(k, 0))
        body(Step(k, 1))
    for i in range(b, last + 1):
        body(Step(i // 2, i % 2))


def gnn_ffn(nc, x, src, dst, w_t, b, base_t, b_low, router_b, out, deg_dram, spill_dram):
    with ExitStack() as ctx:
        def sem(name):
            return ctx.enter_context(nc.semaphore(name))

        def bank(name):
            return ctx.enter_context(nc.psum_tensor(name, [P, HALF], F32))

        base = -(-nc.sbuf_base // 64) * 64
        at = [base]
        size = {F32: 4, F32R: 4, I32: 4, U32: 4, BF16: 2}

        def place(name, shape, dt, offset=None):
            n = size[dt]
            for s in shape[1:]:
                n *= s
            here = at[0] if offset is None else offset
            if offset is None:
                at[0] += -(-n // 32) * 32
            return nc.alloc_sbuf_tensor_at(name, shape, dt, offset=here), here

        def sb(name, shape, dt, offset=None):
            return place(name, shape, dt, offset)[0]

        w_hi = sb("w_hi", [P, KB, D], F32R)
        w_lo, o = place("w_lo", [P, KB, D], F32R)
        w_raw = sb("w_raw", [P, KB, D], F32, o)
        base_hi = sb("base_hi", [P, KB, BCOLS], F32R)
        base_lo, o = place("base_lo", [P, KB, BCOLS], F32R)
        base_raw = sb("base_raw", [P, KB, BCOLS], F32, o)
        bl_hi = sb("bl_hi", [KLOW, D], F32R)
        bl_lo, o = place("bl_lo", [KLOW, D], F32R)
        bl_raw = sb("bl_raw", [KLOW, D], F32, o)

        shared_at = at[0]
        u_hi = sb("u_hi", [P, KB, P], F32R)
        u_lo = sb("u_lo", [P, KB, P], F32R)
        z_hi = sb("z_hi", [P, KB, P], F32R)
        z_lo = sb("z_lo", [P, KB, P], F32R)
        z = sb("z", [P, D], F32)
        y = [sb(f"y{q}", [P, D], F32) for q in range(2)]
        g_hi = sb("g_hi", [P, D], F32R)
        g_lo = sb("g_lo", [P, D], F32R)
        u = sb("u", [P, SPILLW], F32)
        xg = sb("xg", [P, D], F32)
        shared_end = at[0]
        xb = [sb(f"xb{q}", [P, D], F32) for q in range(2)]
        b_rows = sb("b_rows", [P, D], F32)

        ident = sb("ident", [P, P], F32)
        iota = sb("iota", [P, P], F32)
        sel = sb("sel", [P, P], F32R)
        rb_rows = sb("rb_rows", [P, EXPERTS], F32)
        before = sb("before", [P, EXPERTS, EXPERTS], F32)
        slot_row = sb("slot_row", [P, TILES], U32)
        slot_node = sb("slot_node", [P, TILES], F32)
        deg_col = sb("deg_col", [P, TILES], F32)
        tick = sb("tick", [P, 1], F32)
        tick_pool = sb("tick_pool", [P, 4], F32)
        row_now = sb("row_now", [P, 1], U32)
        neg_half = sb("neg_half", [P, 4], F32)
        pin = sb("pin", [P, 4], F32)
        pw = sb("pw", [P, 4], F32)
        st = sb("st", [P, 4, 6], F32)
        mv = sb("mv", [P, 2, 2], F32)
        scale = sb("scale", [P, 2], F32)
        shift = sb("shift", [P, 2], F32)
        dis = [sb(f"dis{q}", [P, 1], F32) for q in range(2)]
        ds = sb("ds", [P, 1], F32)
        sty = sb("sty", [P, 2, 6], F32)
        mvy = sb("mvy", [P, 2], F32)
        piny = sb("piny", [P, 1], F32)
        rstdy = sb("rstdy", [P, 1], F32)
        lg = sb("lg", [P, EXPERTS], F32)
        lg_max = sb("lg_max", [P, 1], F32)
        ex = sb("ex", [P, EXPERTS], F32)
        ex_sum = sb("ex_sum", [P, 1], F32)
        gate = sb("gate", [P, EXPERTS], F32)
        above = sb("above", [P, EXPERTS, EXPERTS], F32)
        tied = sb("tied", [P, EXPERTS, EXPERTS], F32)
        place_of = sb("place_of", [P, EXPERTS], F32)
        wt = sb("wt", [P, EXPERTS], F32)
        wt_sum = sb("wt_sum", [P, 1], F32)
        hs = sb("hs", [P, KLOW], F32)
        hs_hi = sb("hs_hi", [KLOW, P], F32R)
        hs_lo = sb("hs_lo", [KLOW, P], F32R)
        spill_flag = sb("spill_flag", [1, 1], I32)
        spill_row = sb("spill_row", [P, CHUNKS], U32)
        spill_key = sb("spill_key", [P, CHUNKS], F32)
        key_now = sb("key_now", [P, 1], F32)
        lane = sb("lane", [P, 1], F32)
        lane_i = sb("lane_i", [P, 1], I32)
        earlier = sb("earlier", [P, 1], F32)
        target = sb("target", [P, 1], U32)
        spill_diag, spill_ones, same, spill_low = (y[0][:, v * P:(v + 1) * P] for v in range(4))

        slab = at[0] - base
        at[0] = shared_at
        hot_tile = sb("hot_tile", [P, CHUNKS, TILES], BF16)
        hot_local, o = place("hot_local", [P, CHUNKS, P], BF16)
        hot_slot = sb("hot_slot", [P, CHUNKS, P], BF16, o)
        slot_vals, o = place("slot_vals", [P, CHUNKS, 3, TILES], BF16)
        carry = sb("carry", [TILES, CHUNKS, TILES], F32, o)
        prod = sb("prod", [P, GROUP, TILES], F32)
        slots = sb("slots", [P, 3, TILES], F32)
        iota_i = sb("iota_i", [P, P], I32)
        src_i = sb("src_i", [P, CHUNKS], I32)
        dst_i = sb("dst_i", [P, CHUNKS], I32)
        parts_i = sb("parts_i", [P, 4, CHUNKS], I32)
        parts = sb("parts", [P, 4, CHUNKS], F32)
        vals = sb("vals", [P, 3, CHUNKS], F32)
        pos = sb("pos", [P, CHUNKS], F32)
        pos_max = sb("pos_max", [P, 1], F32)
        ones = sb("ones", [P, CHUNKS], F32)
        ones_rows = sb("ones_rows", [TILES, P], F32)
        ones_b = sb("ones_b", [P, 1], BF16)
        low_b = sb("low_b", [P, P], BF16)
        counts = sb("counts", [TILES, CHUNKS], F32)
        sums = sb("sums", [TILES, CHUNKS], F32)
        deg_t = sb("deg_t", [TILES, P], F32)
        assert at[0] <= shared_end, (at[0], shared_end)
        ctx.enter_context(nc.sbuf_tensor("slab", [P, slab // 4 + 16], F32))

        bt = [bank(f"bt{h}") for h in range(2)]
        bg = [bank(f"bg{h}") for h in range(2)]
        bo = [bank(f"bo{v}") for v in range(3)]
        bh = bo[0]
        bm = bank("bm")

        edges_in = sem("edges_in")
        w_in = [sem(f"w_in{k}") for k in range(KB)]
        base_in = [sem(f"base_in{k}") for k in range(KB)]
        bl_in, rows_in = sem("bl_in"), sem("rows_in")
        x_in = [sem(f"x_in{q}") for q in range(2)]
        rows_gathered, degs_gathered = sem("rows_gathered"), sem("degs_gathered")
        deg_stored, out_stored = sem("deg_stored"), sem("out_stored")
        consts, consts_cast, zeroed = sem("consts"), sem("consts_cast"), sem("zeroed")
        w_hi_ok, w_lo_ok, rest_hi_ok, rest_lo_ok = (sem("w_hi_ok"), sem("w_lo_ok"),
                                                    sem("rest_hi_ok"), sem("rest_lo_ok"))
        hot_ok, counts_done, deg_done = sem("hot_ok"), sem("counts_done"), sem("deg_done")
        carry_ok, prefix_done, prefix_used = sem("carry_ok"), sem("prefix_done"), sem("prefix_used")
        deg_ok, slots_hot_ok, slots_done = sem("deg_ok"), sem("slots_hot_ok"), sem("slots_done")
        max_ok, max_done, tables_ok = sem("max_ok"), sem("max_done"), sem("tables_ok")
        edge_chain = sem("edge_chain")
        row_copied, stats_ok, rstd_ok, scales_ok = (sem("row_copied"), sem("stats_ok"),
                                                    sem("rstd_ok"), sem("scales_ok"))
        g_ok, g_hi_ok, g_lo_ok, self_ok, self_full = (sem("g_ok"), sem("g_hi_ok"), sem("g_lo_ok"),
                                                      sem("self_ok"), sem("self_full"))
        sum_done, u_ok, ut_done, u_hi_ok, u_lo_ok = (sem("sum_done"), sem("u_ok"), sem("ut_done"),
                                                     sem("u_hi_ok"), sem("u_lo_ok"))
        prep_chain = sem("prep_chain")
        sum_chain = sem("sum_chain")
        first_done, y_ok, ystats_ok, rstdy_ok, z_ok = (sem("first_done"), sem("y_ok"),
                                                       sem("ystats_ok"), sem("rstdy_ok"),
                                                       sem("z_ok"))
        y_chain = sem("y_chain")
        zt_done, z_hi_ok, z_lo_ok, h_done, logits_ok, exp_ok = (
            sem("zt_done"), sem("z_hi_ok"), sem("z_lo_ok"), sem("h_done"), sem("logits_ok"),
            sem("exp_ok"))
        hs_ok, hst_done, hs_hi_ok, hs_lo_ok, second_done, out_ok = (
            sem("hs_ok"), sem("hst_done"), sem("hs_hi_ok"), sem("hs_lo_ok"), sem("second_done"),
            sem("out_ok"))
        route_chain, route_last, xb_ok = sem("route_chain"), sem("route_last"), sem("xb_ok")

        spill_low_ok, spill_keys_ok, spill_zeroed = (sem("spill_low_ok"), sem("spill_keys_ok"),
                                                     sem("spill_zeroed"))
        spill_zero_ok, spill_copied, spill_in, spill_deg_in = (
            sem("spill_zero_ok"), sem("spill_copied"), sem("spill_in"), sem("spill_deg_in"))
        spill_var_ok, spill_pow_ok, spill_v_ok, spill_diag_ok = (
            sem("spill_var_ok"), sem("spill_pow_ok"), sem("spill_v_ok"), sem("spill_diag_ok"))
        spill_keys_done, spill_same_ok, spill_sum_done, spill_sum_ok = (
            sem("spill_keys_done"), sem("spill_same_ok"), sem("spill_sum_done"),
            sem("spill_sum_ok"))
        spill_added, spill_chain, spill_back, spill_pick = (
            sem("spill_added"), sem("spill_chain"), sem("spill_back"), sem("spill_pick"))

        def rows(t):
            return bass.ds(t * P, P)

        def part(v):
            a = HCOLS if v == 0 else 0
            return (bo[v][:, a:CUTS[v + 1] - CUTS[v]],
                    slice(CUTS[v] + a - HCOLS, CUTS[v + 1] - HCOLS))

        block = ctx.enter_context(nc.Block())

        @block.sync
        def _(sp):
            sp.dma_start(src_i[:], src.rearrange("(p c) -> p c", c=CHUNKS)).then_inc(edges_in, 16)
            sp.dma_start(dst_i[:], dst.rearrange("(p c) -> p c", c=CHUNKS)).then_inc(edges_in, 16)
            for k in range(KB):
                sp.dma_start(w_raw[:, k, :], w_t[k * P:(k + 1) * P, :]).then_inc(w_in[k], 16)
            for q in range(2):
                sp.dma_start(xb[q][:], x[q * P:(q + 1) * P, :]).then_inc(x_in[q], 16)
            sp.dma_start(b_rows[:], b.partition_broadcast(P)).then_inc(rows_in, 16)
            sp.dma_start(rb_rows[:], router_b.partition_broadcast(P)).then_inc(rows_in, 16)
            for k in range(KB):
                sp.dma_start(base_raw[:, k, :], base_t[k * P:(k + 1) * P, :]) \
                    .then_inc(base_in[k], 16)
            sp.dma_start(bl_raw[:], b_low).then_inc(bl_in, 16)
            sp.wait_ge(deg_ok, 1)
            sp.dma_start(deg_dram.rearrange("(t p) a -> t (p a)", p=P), deg_t[:]) \
                .then_inc(deg_stored, 16)

            def step(s):
                if s.has(-2):
                    sp.wait_ge(out_ok, 3 * (s.tile(-2) + 1))
                    sp.dma_start(out[rows(s.tile(-2)), :], y[s.par(-2)][:]).then_inc(out_stored, 16)
                if s.has(2):
                    sp.wait_ge(y_ok, 2 * (s.tile(0) + 1))
                    sp.dma_start(xb[s.par(2)][:], x[rows(s.tile(2)), :]) \
                        .then_inc(x_in[s.par(2)], 16)

            pipeline(sp, step, 0, TILES + 1)
            sp.wait_ge(deg_stored, 16)
            sp.wait_ge(out_stored, 16 * TILES)

        @block.gpsimd
        def _(pool):
            def carry_wait(n):
                nc.gpsimd.tensor_tensor(tick_pool[:, n:n + 1], neg_half[:, 0:1],
                                        neg_half[:, 0:1], ALU.mult)

            nc.gpsimd.memset(ident[:], 0.0).then_inc(zeroed, 1)
            nc.gpsimd.memset(low_b[:], 1.0).then_inc(zeroed, 1)
            nc.gpsimd.memset(before[:], 1.0).then_inc(zeroed, 1)
            nc.gpsimd.iota(iota_i[:], pattern=[[1, P]], base=0, channel_multiplier=0) \
                .then_inc(consts, 1)
            pool.wait_ge(zeroed, 3)
            nc.gpsimd.affine_select(out=ident[:], in_=ident[:], compare_op=ALU.not_equal, fill=1.0,
                                    base=0, pattern=[[-1, P]], channel_multiplier=1) \
                .then_inc(consts, 1)
            nc.gpsimd.affine_select(out=low_b[:], in_=low_b[:], compare_op=ALU.is_gt, fill=0.0,
                                    base=0, pattern=[[1, P]], channel_multiplier=-1) \
                .then_inc(consts, 1)
            nc.gpsimd.affine_select(out=before[:], in_=before[:], compare_op=ALU.is_gt, fill=0.0,
                                    base=0, pattern=[[1, EXPERTS], [-1, EXPERTS]],
                                    channel_multiplier=0).then_inc(consts, 1)
            nc.gpsimd.memset(ones_b[:], 1.0).then_inc(consts, 1)
            nc.gpsimd.memset(ones[:], 1.0).then_inc(consts, 1)
            nc.gpsimd.memset(neg_half[:], -0.5).then_inc(consts, 1)
            nc.gpsimd.memset(pin[:], 1.0).then_inc(consts, 1)
            nc.gpsimd.memset(hs[:], 1.0).then_inc(consts, 1)
            for k in range(KB):
                pool.wait_ge(w_in[k], 16)
                pool.wait_ge(w_hi_ok, k + 1)
                nc.gpsimd.tensor_tensor(w_lo[:, k, :], w_raw[:, k, :], w_hi[:, k, :].bitcast(F32),
                                        ALU.subtract).then_inc(w_lo_ok, 1)
            for k in range(KB):
                pool.wait_ge(base_in[k], 16)
                pool.wait_ge(rest_hi_ok, k + 1)
                nc.gpsimd.tensor_tensor(base_lo[:, k, :], base_raw[:, k, :],
                                        base_hi[:, k, :].bitcast(F32), ALU.subtract) \
                    .then_inc(rest_lo_ok, 1)
            pool.wait_ge(bl_in, 16)
            pool.wait_ge(rest_hi_ok, KB + 1)
            nc.gpsimd.tensor_tensor(bl_lo[:], bl_raw[:], bl_hi[:].bitcast(F32), ALU.subtract) \
                .then_inc(rest_lo_ok, 1)

            def gather(t):
                nc.gpsimd.tensor_copy(row_now[:], slot_row[:, bass.ds(t, 1)]).then_inc(row_copied, 1)
                nc.gpsimd.tensor_copy(pin[:, 2:3], deg_col[:, bass.ds(t, 1)]) \
                    .then_inc(row_copied, 1)
                pool.wait_ge(row_copied, 2 * (t + 1))
                carry_wait(0)
                nc.gpsimd.indirect_dma_start(
                    xg[:], None, x, bass.IndirectOffsetOnAxis(ap=row_now[:, 0:1], axis=0),
                    bounds_check=N - 1, oob_is_err=False).then_inc(rows_gathered, 16)
                nc.gpsimd.indirect_dma_start(
                    pin[:, 3:4], None, deg_dram,
                    bass.IndirectOffsetOnAxis(ap=row_now[:, 0:1], axis=0),
                    bounds_check=N - 1, oob_is_err=False).then_inc(degs_gathered, 16)

            pool.wait_ge(tables_ok, 1)
            pool.wait_ge(deg_stored, 16)
            spills = pool.value_load(spill_flag[0:1, 0:1], min_val=0, max_val=1)
            with pool.If(spills > 0):
                nc.gpsimd.iota(lane_i[:], pattern=[[0, 1]], base=0, channel_multiplier=1) \
                    .then_inc(spill_low_ok, 1)
                nc.gpsimd.memset(spill_low, 1.0).then_inc(spill_low_ok, 1)
                pool.wait_ge(spill_low_ok, 2)
                nc.gpsimd.affine_select(out=spill_low, in_=spill_low, compare_op=ALU.is_gt,
                                        fill=0.0, base=0, pattern=[[-1, P]],
                                        channel_multiplier=1).then_inc(spill_low_ok, 1)
                nc.gpsimd.memset(spill_ones, 1.0).then_inc(spill_low_ok, 1)
                pool.wait_ge(spill_keys_ok, 1)
                nc.gpsimd.memset(u[:], 0.0).then_inc(spill_zeroed, 1)
                nc.gpsimd.memset(xg[:], 0.0).then_inc(spill_zeroed, 1)
                pool.wait_ge(spill_zeroed, 2)
                with pool.Fori(0, TILES + 1) as t:
                    pool.dma_start(spill_dram[rows(t), :], u[:]).then_inc(spill_zero_ok, 16)
                pool.wait_ge(spill_zero_ok, 16 * (TILES + 1))
                pool.wait_ge(deg_stored, 16)
                with pool.Fori(0, CHUNKS) as c:
                    nc.gpsimd.tensor_copy(row_now[:], spill_row[:, bass.ds(c, 1)]) \
                        .then_inc(spill_copied, 1)
                    pool.wait_ge(spill_copied, c + 1)
                    carry_wait(1)
                    nc.gpsimd.indirect_dma_start(
                        xg[:], None, x, bass.IndirectOffsetOnAxis(ap=row_now[:, 0:1], axis=0),
                        bounds_check=N - 1, oob_is_err=False).then_inc(spill_in, 16)
                    nc.gpsimd.indirect_dma_start(
                        pin[:, 3:4], None, deg_dram,
                        bass.IndirectOffsetOnAxis(ap=row_now[:, 0:1], axis=0),
                        bounds_check=N - 1, oob_is_err=False).then_inc(spill_deg_in, 16)
                    pool.wait_ge(spill_deg_in, 16 * (c + 1))
                    pool.wait_ge(spill_var_ok, c + 1)
                    nc.gpsimd.tensor_tensor(pw[:], pin[:], neg_half[:], ALU.pow) \
                        .then_inc(spill_pow_ok, 1)
                    pool.wait_ge(spill_sum_ok, 2 * (c + 1))
                    carry_wait(2)
                    nc.gpsimd.indirect_dma_start(
                        spill_dram, bass.IndirectOffsetOnAxis(ap=target[:, 0:1], axis=0), u[:],
                        None, bounds_check=NPAD + P - 1, oob_is_err=True, compute_op=ALU.add) \
                        .then_inc(spill_added, 16)
                    pool.wait_ge(spill_added, 16 * (c + 1))
            nc.gpsimd.memset(xg[:], 0.0).then_inc(consts, 1)
            pool.wait_ge(consts, 10)
            gather(0)

            def step(s):
                if s.has(1):
                    n = s.tile(1)
                    pool.wait_ge(degs_gathered, 16 * (n + 1))
                    pool.wait_ge(stats_ok, n + 1)
                    if not (isinstance(n, int) and n == 0):
                        pool.wait_ge(scales_ok, n)
                        pool.wait_ge(sum_done, n)
                    nc.gpsimd.tensor_tensor(pw[:], pin[:], neg_half[:], ALU.pow) \
                        .then_inc(rstd_ok, 1)
                if s.has(2):
                    f = s.tile(2)
                    pool.wait_ge(g_hi_ok, f)
                    pool.wait_ge(g_lo_ok, 2 * f)
                    pool.wait_ge(rstd_ok, f)
                    gather(f)
                if s.has(1):
                    n = s.tile(1)
                    pool.wait_ge(self_ok, 2 * (n + 1))
                    carry_wait(3)
                    with pool.If(spills > 0):
                        pool.dma_start(u[:], spill_dram[rows(n), :], accum_op=ALU.add) \
                            .then_inc(spill_back, 16)
                        pool.wait_ge(spill_back, 16 * (n + 1))
                    pool.sem_inc(self_full, 1)
                if s.has(0):
                    c = s.tile(0)
                    pool.wait_ge(ystats_ok, c + 1)
                    nc.gpsimd.tensor_tensor(rstdy[:], piny[:], neg_half[:, 0:1], ALU.pow) \
                        .then_inc(rstdy_ok, 1)

            pipeline(pool, step, -1, TILES - 1)

        @block.scalar
        def _(act):
            for k in range(KB):
                act.wait_ge(w_in[k], 16)
                nc.scalar.activation(w_hi[:, k, :], w_raw[:, k, :], ACT.Copy).then_inc(w_hi_ok, 1)
            for k in range(KB):
                act.wait_ge(base_in[k], 16)
                nc.scalar.activation(base_hi[:, k, :], base_raw[:, k, :], ACT.Copy) \
                    .then_inc(rest_hi_ok, 1)
            act.wait_ge(bl_in, 16)
            nc.scalar.activation(bl_hi[:], bl_raw[:], ACT.Copy).then_inc(rest_hi_ok, 1)

            def prepare(s):
                n = s.tile(1)
                first = isinstance(n, int) and n == 0
                act.wait_ge(g_ok, n + 1)
                if not first:
                    act.wait_ge(sum_done, n)
                nc.scalar.activation(g_hi[:], xg[:], ACT.Copy).then_inc(g_hi_ok, 1)
                act.wait_ge(scales_ok, n + 1)
                if not first:
                    act.wait_ge(ut_done, 2 * n)
                nc.scalar.activation(u[:, 0:D], xb[s.par(1)][:], ACT.Identity,
                                     bias=shift[:, 0:1], scale=scale[:, 0:1]).then_inc(self_ok, 1)
                nc.scalar.activation(u[:, D:D + 1], dis[s.par(1)][:], ACT.Copy) \
                    .then_inc(self_ok, 1)

            def step(s):
                if s.has(-1):
                    p = s.tile(-1)
                    for h in range(2):
                        act.wait_ge(zt_done, 2 * p + h + 1)
                        if h == 0 and s.has(-2):
                            act.wait_ge(second_done, 3 * p)
                        nc.scalar.activation(z_hi[:, 4 * h:4 * h + 4, :],
                                             bt[h][:].rearrange("p (k n) -> p k n", n=P),
                                             ACT.Copy).then_inc(z_hi_ok, 1)
                if s.has(1):
                    prepare(s)
                if s.has(-1):
                    act.wait_ge(logits_ok, p + 1)
                    nc.scalar.activation(ex[:], lg[:], ACT.Exp, accum_out=ex_sum[:]) \
                        .then_inc(exp_ok, 1)
                if s.has(1):
                    n = s.tile(1)
                    for h in range(2):
                        act.wait_ge(ut_done, 2 * n + h + 1)
                        if h == 0 and s.has(0):
                            act.wait_ge(first_done, 2 * n)
                        nc.scalar.activation(u_hi[:, 4 * h:4 * h + 4, :],
                                             bt[h][:].rearrange("p (k n) -> p k n", n=P),
                                             ACT.Copy).then_inc(u_hi_ok, 1)
                if s.has(-1):
                    p = s.tile(-1)
                    act.wait_ge(hst_done, p + 1)
                    nc.scalar.activation(hs_hi[:], bm[0:KLOW, 0:P], ACT.Copy).then_inc(hs_hi_ok, 1)

            pipeline(act, step, -1, TILES)

        @block.tensor
        def _(pe):
            pe.wait_ge(hot_ok, 1)
            pe.wait_ge(consts, 9)
            for c in range(CHUNKS):
                last = nc.tensor.matmul(bo[2][0:TILES, c:c + 1], hot_tile[:, c, :], ones_b[:],
                                        start=True, stop=True)
            last.then_inc(counts_done, 1)
            pe.wait_ge(hot_ok, 2)
            for c in range(CHUNKS):
                nc.tensor.matmul(bh[0:TILES, 0:P], hot_tile[:, c, :], hot_local[:, c, :],
                                 start=(c == 0), stop=(c == CHUNKS - 1)).then_inc(deg_done, 1)
            for c in range(CHUNKS):
                nc.tensor.matmul(bm[:, 0:TILES], hot_local[:, c, :], hot_tile[:, c, :],
                                 start=(c == 0), stop=(c == CHUNKS - 1)).then_inc(deg_done, 1)
            pe.wait_ge(carry_ok, 1)
            banks = [bt[0], bt[1], bg[0], bg[1]]
            for g in range(GROUPS):
                c0, c1 = g * GROUP, min((g + 1) * GROUP, CHUNKS)
                if g >= len(banks):
                    pe.wait_ge(prefix_used, g - len(banks) + 1)
                ps = banks[g % len(banks)][:, 0:(c1 - c0) * TILES]
                nc.tensor.matmul(ps, low_b[:], hot_tile[:, c0:c1, :].rearrange("p c t -> p (c t)"),
                                 start=True, stop=False)
                pe.wait_ge(consts_cast, 2)
                nc.tensor.matmul(ps, ones_rows[:],
                                 carry[:, c0:c1, :].rearrange("p c t -> p (c t)"),
                                 start=False, stop=True).then_inc(prefix_done, 1)
            for c in range(CHUNKS):
                if c % GROUP == 0:
                    pe.wait_ge(slots_hot_ok, c // GROUP + 1)
                last = nc.tensor.matmul(bo[1][:, 0:3 * TILES], hot_slot[:, c, :],
                                        slot_vals[:, c, :, :].rearrange("p v t -> p (v t)"),
                                        start=(c == 0), stop=(c == CHUNKS - 1))
            last.then_inc(slots_done, 1)
            pe.wait_ge(max_ok, 1)
            nc.tensor.transpose(bo[2][0:1, 0:P], pos_max[:], ident[:]).then_inc(max_done, 1)

            pe.wait_ge(tables_ok, 1)
            spills = pe.value_load(spill_flag[0:1, 0:1], min_val=0, max_val=1)
            with pe.If(spills > 0):
                pe.wait_ge(spill_low_ok, 4)
                with pe.Fori(0, CHUNKS) as c:
                    pe.wait_ge(spill_diag_ok, c + 1)
                    nc.tensor.matmul(bm[:, 0:P], spill_ones, spill_diag, start=True, stop=True) \
                        .then_inc(spill_keys_done, 1)
                    pe.wait_ge(spill_v_ok, c + 1)
                    pe.wait_ge(spill_same_ok, c + 1)
                    for h in range(2):
                        nc.tensor.matmul(bt[h][:], same, u[:, h * HALF:(h + 1) * HALF],
                                         start=True, stop=True)
                    nc.tensor.matmul(bh[:, 0:1], same, u[:, D:D + 1], start=True, stop=True) \
                        .then_inc(spill_sum_done, 1)

            def product(ps, hi, lo, m_hi, m_lo, n, ends):
                for k in range(KB):
                    nc.tensor.matmul(ps, hi[:, k, :], m_hi[:, k, n], start=(k == 0), stop=False)
                    nc.tensor.matmul(ps, hi[:, k, :], m_lo[:, k, n], start=False, stop=False)
                    last = nc.tensor.matmul(ps, lo[:, k, :], m_hi[:, k, n], start=False,
                                            stop=(ends and k == KB - 1))
                return last

            def transposes(of, done):
                for h in range(2):
                    for k in range(4):
                        last = nc.tensor.transpose(bt[h][:, k * P:(k + 1) * P],
                                                   of[:, (4 * h + k) * P:(4 * h + k + 1) * P],
                                                   ident[:])
                    last.then_inc(done, 1)

            def step(s):
                if s.has(0):
                    c = s.tile(0)
                    pe.wait_ge(u_hi_ok, 2 * (c + 1))
                    pe.wait_ge(u_lo_ok, 2 * (c + 1))
                    if not s.has(-1):
                        pe.wait_ge(w_hi_ok, KB)
                        pe.wait_ge(w_lo_ok, KB)
                    else:
                        pe.wait_ge(y_ok, 2 * c)
                    product(bg[0][:], u_hi, u_lo, w_hi, w_lo, slice(0, HALF), True) \
                        .then_inc(first_done, 1)
                if s.has(-1):
                    p = s.tile(-1)
                    pe.wait_ge(z_ok, p + 1)
                    transposes(z, zt_done)
                if s.has(0):
                    product(bg[1][:], u_hi, u_lo, w_hi, w_lo, slice(HALF, D), True) \
                        .then_inc(first_done, 1)
                if s.has(1):
                    n = s.tile(1)
                    pe.wait_ge(g_hi_ok, n + 1)
                    pe.wait_ge(g_lo_ok, 2 * (n + 1))
                    if s.has(-1):
                        pe.wait_ge(z_lo_ok, 2 * s.tile(0))
                    if s.has(-2):
                        pe.wait_ge(hs_lo_ok, s.tile(-1))
                    for h in range(2):
                        half = slice(h * HALF, (h + 1) * HALF)
                        nc.tensor.matmul(bt[h][:], sel[:], g_hi[:, half], start=True, stop=False)
                        nc.tensor.matmul(bt[h][:], sel[:], g_lo[:, half], start=False, stop=True)
                    nc.tensor.matmul(bm[:, HALF - 2:HALF - 1], sel[:].bitcast(F32), pw[:, 3:4],
                                     start=True, stop=True).then_inc(sum_done, 1)

                def second(v):
                    c0, c1 = CUTS[v], CUTS[v + 1]
                    return product(bo[v][:, 0:c1 - c0], z_hi, z_lo, base_hi, base_lo,
                                   slice(c0, c1), True)

                if s.has(-1):
                    p = s.tile(-1)
                    pe.wait_ge(z_hi_ok, 2 * (p + 1))
                    pe.wait_ge(z_lo_ok, 2 * (p + 1))
                    if not s.has(-2):
                        pe.wait_ge(rest_hi_ok, KB + 1)
                        pe.wait_ge(rest_lo_ok, KB + 1)
                    else:
                        pe.wait_ge(out_ok, 3 * p)
                        pe.wait_ge(hs_ok, p)
                    second(0).then_inc(h_done, 1)
                if s.has(1):
                    pe.wait_ge(u_ok, s.tile(1) + 1)
                    transposes(u, ut_done)
                if s.has(-1):
                    p = s.tile(-1)
                    second(1)
                    pe.wait_ge(hs_ok, p + 1)
                    nc.tensor.transpose(bm[0:KLOW, 0:P], hs[:], ident[:]).then_inc(hst_done, 1)
                    second(2)
                    pe.wait_ge(hs_hi_ok, p + 1)
                    pe.wait_ge(hs_lo_ok, p + 1)
                    for v in range(3):
                        ps, cols = part(v)
                        nc.tensor.matmul(ps, hs_hi[:], bl_hi[:, cols], start=False, stop=False,
                                         skip_group_check=True)
                        nc.tensor.matmul(ps, hs_hi[:], bl_lo[:, cols], start=False, stop=False,
                                         skip_group_check=True)
                        nc.tensor.matmul(ps, hs_lo[:], bl_hi[:, cols], start=False, stop=True,
                                         skip_group_check=True).then_inc(second_done, 1)

            pipeline(pe, step, -1, TILES)

        @block.vector
        def _(dve):
            edge = Chain(edge_chain, 10 ** 6)
            edge.start(0)

            def link(ins):
                edge.link(dve, ins)

            dve.wait_ge(consts, 9)
            nc.vector.memset(ones_rows[:], 1.0).then_inc(consts_cast, 1)
            nc.vector.tensor_copy(iota[:], iota_i[:]).then_inc(consts_cast, 1)
            dve.wait_ge(edges_in, 32)
            for v, (of, op, by) in enumerate([(src_i, ALU.logical_shift_right, 7),
                                              (src_i, ALU.bitwise_and, P - 1),
                                              (dst_i, ALU.logical_shift_right, 7),
                                              (dst_i, ALU.bitwise_and, P - 1)]):
                link(nc.vector.tensor_scalar(parts_i[:, v, :], of[:], by, None, op))
            link(nc.vector.tensor_copy(parts[:], parts_i[:]))
            dve.wait_ge(consts_cast, 2)

            def hot(o, of, width, chunks=CHUNKS):
                return nc.vector.tensor_tensor(
                    o, of.unsqueeze(2).to_broadcast([P, chunks, width]),
                    iota[:, 0:width].unsqueeze(1).to_broadcast([P, chunks, width]), ALU.is_equal)

            hot(hot_tile[:], parts[:, 0, :], TILES).then_inc(hot_ok, 1)
            hot(hot_local[:], parts[:, 1, :], P).then_inc(hot_ok, 1)
            dve.wait_ge(counts_done, 1)
            link(nc.vector.tensor_copy(counts[:], bo[2][0:TILES, 0:CHUNKS]))
            link(nc.vector.tensor_tensor_scan(sums[:], ones[0:TILES, :], counts[:], 0.0, ALU.mult,
                                              ALU.add))
            link(nc.vector.tensor_tensor(sums[:], sums[:], counts[:], ALU.subtract))
            nc.vector.tensor_tensor(
                carry[:], ident[0:TILES, 0:TILES].unsqueeze(1).to_broadcast([TILES, CHUNKS, TILES]),
                sums[:].unsqueeze(2).to_broadcast([TILES, CHUNKS, TILES]), ALU.mult) \
                .then_inc(carry_ok, 1)
            dve.wait_ge(deg_done, 2 * CHUNKS)
            nc.vector.tensor_scalar(deg_t[:], bh[0:TILES, 0:P], 1.0, None, ALU.add) \
                .then_inc(deg_ok, 1)
            nc.vector.tensor_scalar(deg_col[:], bm[:, 0:TILES], 1.0, None, ALU.add) \
                .then_inc(deg_ok, 1)
            banks = [bt[0], bt[1], bg[0], bg[1]]
            dve.wait_ge(hot_ok, 2)
            for g in range(GROUPS):
                c0, c1 = g * GROUP, min((g + 1) * GROUP, CHUNKS)
                dve.wait_ge(prefix_done, g + 1)
                ps = banks[g % len(banks)][:, 0:(c1 - c0) * TILES]
                ins = nc.vector.tensor_tensor(prod[:, 0:c1 - c0, :],
                                              ps.rearrange("p (c t) -> p c t", t=TILES),
                                              hot_tile[:, c0:c1, :], ALU.mult)
                ins.then_inc(prefix_used, 1)
                dve.wait_ge(prefix_used, g + 1)
                link(nc.vector.tensor_reduce(pos[:, c0:c1], prod[:, 0:c1 - c0, :], AX.X, ALU.add))
            nc.vector.tensor_reduce(pos_max[:], pos[:], AX.X, ALU.max).then_inc(max_ok, 1)
            link(nc.vector.tensor_scalar(vals[:, 0, :], parts[:, 2, :], 1.0, None, ALU.add))
            link(nc.vector.tensor_copy(vals[:, 1, :], parts[:, 3, :]))
            link(nc.vector.tensor_scalar(vals[:, 2, :], parts[:, 1, :], 1.0, None, ALU.add))
            for v in range(3):
                link(nc.vector.tensor_tensor(
                    slot_vals[:, :, v, :], hot_tile[:],
                    vals[:, v, :].unsqueeze(2).to_broadcast([P, CHUNKS, TILES]), ALU.mult))
            for c0 in range(0, CHUNKS, GROUP):
                c1 = min(c0 + GROUP, CHUNKS)
                hot(hot_slot[:, c0:c1, :], pos[:, c0:c1], P, c1 - c0).then_inc(slots_hot_ok, 1)
            dve.wait_ge(slots_done, 1)
            link(nc.vector.tensor_copy(slots[:], bo[1][:, 0:3 * TILES]
                                       .rearrange("p (v t) -> p v t", t=TILES)))
            link(nc.vector.scalar_tensor_tensor(slots[:, 0, :], slots[:, 0, :], float(P),
                                                slots[:, 1, :], ALU.mult, ALU.add))
            link(nc.vector.tensor_scalar(slots[:, 1, :], slots[:, 0, :], float(P), float(FAR),
                                         ALU.is_lt, ALU.mult))
            link(nc.vector.scalar_tensor_tensor(slot_row[:], slots[:, 0, :], -float(P),
                                                slots[:, 1, :], ALU.add, ALU.add))
            link(nc.vector.tensor_scalar(slot_node[:], slots[:, 2, :], -1.0, None, ALU.add))
            dve.wait_ge(max_done, 1)
            link(nc.vector.tensor_reduce(pos_max[0:1, :], bo[2][0:1, 0:P], AX.X, ALU.max))
            nc.vector.tensor_scalar(spill_flag[:], pos_max[0:1, :], float(P), None, ALU.is_ge) \
                .then_inc(tables_ok, 1)

            dve.wait_ge(tables_ok, 1)
            spills = dve.value_load(spill_flag[0:1, 0:1], min_val=0, max_val=1)
            with dve.If(spills > 0):
                spill = Chain(spill_chain, 6)
                link(nc.vector.scalar_tensor_tensor(parts[:, 1, :], parts[:, 0, :], float(P),
                                                    parts[:, 1, :], ALU.mult, ALU.add))
                link(nc.vector.scalar_tensor_tensor(parts[:, 3, :], parts[:, 2, :], float(P),
                                                    parts[:, 3, :], ALU.mult, ALU.add))
                link(nc.vector.tensor_scalar(pos[:], pos[:], float(P), None, ALU.is_ge))
                dve.wait_ge(spill_low_ok, 4)
                link(nc.vector.tensor_copy(lane[:], lane_i[:]))
                link(nc.vector.tensor_scalar(parts[:, 1, :], parts[:, 1, :], lane[:], 1.0, ALU.add,
                                             ALU.add))
                link(nc.vector.tensor_tensor(parts[:, 1, :], parts[:, 1, :], pos[:], ALU.mult))
                link(nc.vector.tensor_scalar(spill_key[:], parts[:, 1, :], lane[:], 1.0,
                                             ALU.subtract, ALU.subtract))
                link(nc.vector.scalar_tensor_tensor(parts[:, 3, :], parts[:, 3, :], -float(FAR),
                                                    pos[:], ALU.add, ALU.mult))
                nc.vector.tensor_scalar(spill_row[:], parts[:, 3, :], float(FAR), None, ALU.add) \
                    .then_inc(spill_keys_ok, 1)
                with dve.Fori(0, CHUNKS) as c:
                    spill.start(c)
                    spill.link(dve, nc.vector.tensor_copy(key_now[:], spill_key[:, bass.ds(c, 1)]))
                    nc.vector.tensor_scalar(spill_diag, ident[:], key_now[:], None, ALU.mult) \
                        .then_inc(spill_diag_ok, 1)
                    dve.wait_ge(spill_in, 16 * (c + 1))
                    for h in range(2):
                        ins = nc.vector.bn_stats(st[:, h, :], xg[:, h * HALF:(h + 1) * HALF])
                    spill.link(dve, ins)
                    nc.vector.memset(tick[:], 0.0)
                    spill.link(dve, nc.vector.bn_aggr(
                        mv[:, 1, :], st[:, 0:2, :].rearrange("p a b -> p (a b)")))
                    nc.vector.tensor_scalar(pin[:, 1:2], mv[:, 1, 1:2], LN_EPS, None, ALU.add) \
                        .then_inc(spill_var_ok, 1)
                    dve.wait_ge(spill_pow_ok, c + 1)
                    spill.link(dve, nc.vector.tensor_tensor(scale[:, 1:2], pw[:, 1:2], pw[:, 3:4],
                                                            ALU.mult))
                    nc.vector.tensor_scalar(u[:, 0:D], xg[:], mv[:, 1, 0:1], scale[:, 1:2],
                                            ALU.subtract, ALU.mult)
                    nc.vector.tensor_copy(u[:, D:D + 1], pw[:, 3:4]).then_inc(spill_v_ok, 1)
                    dve.wait_ge(spill_keys_done, c + 1)
                    nc.vector.tensor_scalar(same, bm[:, 0:P], key_now[:], None, ALU.is_equal) \
                        .then_inc(spill_same_ok, 1)
                    dve.wait_ge(spill_same_ok, c + 1)
                    spill.link(dve, nc.vector.tensor_tensor(spill_diag, same, spill_low, ALU.mult))
                    spill.link(dve, nc.vector.tensor_reduce(earlier[:], spill_diag, AX.X, ALU.add))
                    spill.end()
                    pick = Chain(spill_pick, 5)
                    pick.start(c)
                    pick.link(dve, nc.vector.tensor_scalar(earlier[:], earlier[:], 0.5, None,
                                                           ALU.is_lt))
                    pick.link(dve, nc.vector.scalar_tensor_tensor(
                        earlier[:], key_now[:], 0.0, earlier[:], ALU.is_ge, ALU.mult))
                    pick.link(dve, nc.vector.tensor_scalar(key_now[:], key_now[:], lane[:],
                                                           float(NPAD), ALU.subtract,
                                                           ALU.subtract))
                    pick.link(dve, nc.vector.tensor_tensor(key_now[:], key_now[:], earlier[:],
                                                           ALU.mult))
                    nc.vector.tensor_scalar(target[:], key_now[:], lane[:], float(NPAD), ALU.add,
                                            ALU.add).then_inc(spill_sum_ok, 1)
                    dve.wait_ge(spill_sum_done, c + 1)
                    for h in range(2):
                        nc.vector.tensor_copy(u[:, h * HALF:(h + 1) * HALF], bt[h][:])
                    pick.link(dve, nc.vector.tensor_copy(u[:, D:D + 1], bh[:, 0:1]))
                    pick.end()
                    nc.vector.memset(tick[:], 0.0).then_inc(spill_sum_ok, 1)

            prep = Chain(prep_chain, 6)
            sums_c = Chain(sum_chain, 1)
            yc = Chain(y_chain, 3)
            route = Chain(route_chain, 12)

            def prepare_scales(s):
                n = s.tile(1)
                prep.start(n)
                xt = xb[s.par(1)]
                dve.wait_ge(x_in[s.par(1)], 16 * (s.half(1) + 1))
                for h in range(2):
                    prep.link(dve, nc.vector.bn_stats(st[:, h, :], xt[:, h * HALF:(h + 1) * HALF]))
                dve.wait_ge(rows_gathered, 16 * (n + 1))
                for h in range(2):
                    prep.link(dve, nc.vector.bn_stats(st[:, 2 + h, :],
                                                      xg[:, h * HALF:(h + 1) * HALF]))
                nc.vector.memset(tick[:], 0.0)
                nc.vector.bn_aggr(mv[:, 0, :], st[:, 0:2, :].rearrange("p a b -> p (a b)"))
                prep.link(dve, nc.vector.bn_aggr(mv[:, 1, :],
                                                 st[:, 2:4, :].rearrange("p a b -> p (a b)")))
                nc.vector.tensor_scalar(pin[:, 0:2], mv[:, :, 1], LN_EPS, None, ALU.add) \
                    .then_inc(stats_ok, 1)
                dve.wait_ge(rstd_ok, n + 1)
                if s.has(0):
                    dve.wait_ge(self_ok, 2 * n)
                prep.link(dve, nc.vector.tensor_tensor(scale[:], pw[:, 0:2], pw[:, 2:4], ALU.mult))
                nc.vector.tensor_copy(dis[s.par(1)][:], pw[:, 2:3])
                nc.vector.scalar_tensor_tensor(shift[:], mv[:, :, 0], -1.0, scale[:], ALU.mult,
                                               ALU.mult).then_inc(scales_ok, 1)
                prep.end()
                dve.wait_ge(scales_ok, n + 1)
                nc.vector.tensor_scalar(xg[:], xg[:], scale[:, 1:2], shift[:, 1:2], ALU.mult,
                                        ALU.add).then_inc(g_ok, 1)

            def prepare_low(s):
                n = s.tile(1)
                if s.has(0):
                    dve.wait_ge(sum_done, n)
                nc.vector.tensor_scalar(sel[:], iota[:], slot_node[:, bass.ds(n, 1)], None,
                                        ALU.is_equal).then_inc(g_lo_ok, 1)
                dve.wait_ge(g_hi_ok, n + 1)
                nc.vector.tensor_tensor(g_lo[:], xg[:], g_hi[:].bitcast(F32), ALU.subtract) \
                    .then_inc(g_lo_ok, 1)

            def low_parts(s, a, hi, lo, hi_ok, lo_ok):
                for h in range(2):
                    dve.wait_ge(hi_ok, 2 * s.tile(a) + h + 1)
                    nc.vector.tensor_tensor(lo[:, 4 * h:4 * h + 4, :],
                                            bt[h][:].rearrange("p (k n) -> p k n", n=P),
                                            hi[:, 4 * h:4 * h + 4, :].bitcast(F32),
                                            ALU.subtract).then_inc(lo_ok, 1)

            def finish(s):
                t = s.tile(-2)
                for v in range(3):
                    ps, cols = part(v)
                    dve.wait_ge(second_done, 3 * t + v + 1)
                    yv = y[s.par(-2)][:, cols]
                    nc.vector.tensor_tensor(yv, ps, yv, ALU.add).then_inc(out_ok, 1)

            def make_y(s):
                c = s.tile(0)
                yc.start(c)
                if s.has(-2):
                    dve.wait_ge(out_stored, 16 * (c - 1))
                for h in range(2):
                    half = slice(h * HALF, (h + 1) * HALF)
                    dve.wait_ge(first_done, 2 * c + h + 1)
                    nc.vector.scalar_tensor_tensor(y[s.par(0)][:, half], bg[h][:], dis[s.par(0)][:],
                                                   xb[s.par(0)][:, half], ALU.mult, ALU.add) \
                        .then_inc(y_ok, 1)
                    dve.wait_ge(y_ok, 2 * c + h + 1)
                    yc.link(dve, nc.vector.bn_stats(sty[:, h, :], y[s.par(0)][:, half]))
                nc.vector.memset(tick[:], 0.0)
                yc.link(dve, nc.vector.bn_aggr(mvy[:], sty[:].rearrange("p a b -> p (a b)")))
                nc.vector.tensor_scalar(piny[:], mvy[:, 1:2], LN_EPS, None, ALU.add) \
                    .then_inc(ystats_ok, 1)
                yc.end()

            def make_z(s):
                c = s.tile(0)
                dve.wait_ge(rstdy_ok, c + 1)
                nc.vector.tensor_scalar(z[:], y[s.par(0)][:], mvy[:, 0:1], rstdy[:], ALU.subtract,
                                        ALU.mult).then_inc(z_ok, 1)


            def choose(s):
                p = s.tile(-1)
                route.start(p)
                dve.wait_ge(h_done, p + 1)
                route.link(dve, nc.vector.tensor_tensor(lg[:], bh[:, LOGITS:HCOLS], rb_rows[:],
                                                        ALU.add))
                route.link(dve, nc.vector.tensor_reduce(lg_max[:], lg[:], AX.X, ALU.max))
                nc.vector.tensor_scalar(lg[:], lg[:], lg_max[:], None, ALU.subtract) \
                    .then_inc(logits_ok, 1)
                dve.wait_ge(exp_ok, p + 1)
                route.link(dve, nc.vector.reciprocal(ex_sum[:], ex_sum[:]))
                route.link(dve, nc.vector.tensor_scalar(gate[:], ex[:], ex_sum[:], None, ALU.mult))
                sq = [P, EXPERTS, EXPERTS]
                other, own = (gate[:].unsqueeze(1).to_broadcast(sq),
                              gate[:].unsqueeze(2).to_broadcast(sq))
                route.link(dve, nc.vector.tensor_tensor(above[:], other, own, ALU.is_gt))
                route.link(dve, nc.vector.tensor_tensor(tied[:], other, own, ALU.is_equal))
                route.link(dve, nc.vector.tensor_tensor(tied[:], tied[:], before[:], ALU.mult))
                route.link(dve, nc.vector.tensor_tensor(above[:], above[:], tied[:], ALU.add))
                route.link(dve, nc.vector.tensor_reduce(place_of[:], above[:], AX.X, ALU.add))
                route.link(dve, nc.vector.scalar_tensor_tensor(
                    wt[:], place_of[:], float(TOPK), gate[:], ALU.is_lt, ALU.mult,
                    accum_out=wt_sum[:]))
                route.link(dve, nc.vector.tensor_scalar(wt_sum[:], wt_sum[:], GATE_EPS, None,
                                                        ALU.add))
                route.link(dve, nc.vector.reciprocal(wt_sum[:], wt_sum[:]))
                route.end()
                nc.vector.tensor_scalar(wt[:], wt[:], wt_sum[:], None, ALU.mult) \
                    .then_inc(route_last, 1)
                nc.vector.tensor_copy(hs[:, 0:ROUTED], bh[:, 0:ROUTED])
                dve.wait_ge(route_last, p + 1)
                nc.vector.tensor_tensor(
                    hs[:, ROUTED:LOGITS].rearrange("p (e r) -> p e r", r=RANK),
                    bh[:, ROUTED:LOGITS].rearrange("p (e r) -> p e r", r=RANK),
                    wt[:].unsqueeze(2).to_broadcast([P, EXPERTS, RANK]), ALU.mult) \
                    .then_inc(hs_ok, 1)

            def add_sum(s):
                n = s.tile(1)
                sums_c.start(n)
                dve.wait_ge(self_full, n + 1)
                dve.wait_ge(sum_done, n + 1)
                sums_c.link(dve, nc.vector.tensor_scalar(
                    ds[:], bm[:, HALF - 2:HALF - 1], u[:, D:D + 1], dis[s.par(1)][:], ALU.add,
                    ALU.mult))
                for h in range(2):
                    half = slice(h * HALF, (h + 1) * HALF)
                    ins = nc.vector.tensor_tensor(u[:, half], bt[h][:], u[:, half], ALU.add)
                ins.then_inc(u_ok, 1)
                nc.vector.scalar_tensor_tensor(xb[s.par(1)][:], b_rows[:], ds[:], xb[s.par(1)][:],
                                               ALU.mult, ALU.add).then_inc(xb_ok, 1)
                sums_c.end()

            def step(s):
                if s.has(-2):
                    finish(s)
                if s.has(1):
                    prepare_scales(s)
                if s.has(-1):
                    low_parts(s, -1, z_hi, z_lo, z_hi_ok, z_lo_ok)
                if s.has(1):
                    prepare_low(s)
                if s.has(0):
                    dve.wait_ge(xb_ok, s.tile(0) + 1)
                    make_y(s)
                if s.has(1):
                    if not s.has(0):
                        dve.wait_ge(rows_in, 32)
                    add_sum(s)
                if s.has(0):
                    make_z(s)
                if s.has(-1):
                    choose(s)
                if s.has(1):
                    low_parts(s, 1, u_hi, u_lo, u_hi_ok, u_lo_ok)
                if s.has(-1):
                    p = s.tile(-1)
                    dve.wait_ge(hs_hi_ok, p + 1)
                    nc.vector.tensor_tensor(hs_lo[:], bm[0:KLOW, 0:P], hs_hi[:].bitcast(F32),
                                            ALU.subtract).then_inc(hs_lo_ok, 1)

            pipeline(dve, step, -1, TILES + 1)


def kernel(x, src, dst, L0_gnn_W, L0_gnn_b, L0_ffn_base_W, L0_ffn_base_b, L0_ffn_shared_A,
           L0_ffn_shared_B, L0_ffn_routed_A, L0_ffn_routed_B, L0_ffn_router_W, L0_ffn_router_b):
    import numpy as np
    import concourse.bacc as bacc
    from concourse.bass_utils import run_bass_kernel_spmd

    def padded(a, n, fill):
        p = np.full((n,) + a.shape[1:], fill, a.dtype)
        p[:a.shape[0]] = a
        return p

    a = np.asarray
    arrays = {
        "x": padded(a(x), NPAD, 0),
        "src": padded(a(src), EPAD, NPAD),
        "dst": padded(a(dst), EPAD, 0),
        "w_t": np.ascontiguousarray(a(L0_gnn_W).T),
        "b": a(L0_gnn_b),
        "base_t": np.ascontiguousarray(np.concatenate(
            [a(L0_ffn_shared_A), a(L0_ffn_routed_A).reshape(EXPERTS * RANK, D),
             a(L0_ffn_router_W), a(L0_ffn_base_W)]).T),
        "b_low": np.ascontiguousarray(np.concatenate(
            [a(L0_ffn_shared_B).T, a(L0_ffn_routed_B).transpose(0, 2, 1).reshape(-1, D),
             a(L0_ffn_base_b)[None]])),
        "router_b": a(L0_ffn_router_b),
    }
    nc = bacc.Bacc("TRN2", target_bir_lowering=False, num_devices=1)
    aps = [nc.dram_tensor(n, v.shape, mybir.dt.from_np(v.dtype), kind="ExternalInput").ap()
           for n, v in arrays.items()]
    out = nc.dram_tensor("out", (NPAD, D), F32, kind="ExternalOutput").ap()
    deg = nc.dram_tensor("deg", (NPAD, 1), F32).ap()
    spill = nc.dram_tensor("spill", (NPAD + P, SPILLW), F32).ap()
    gnn_ffn(nc, *aps, out, deg, spill)
    r = run_bass_kernel_spmd(nc, [arrays], core_ids=[0])
    return r.results[0]["out"][:N]
```
